# Optimizing a Trainium2 kernel written in Bass

```python
import numpy as np
import jax
import jax.numpy as jnp

def _softmax(x, axis=-1):
    return jax.nn.softmax(x, axis=axis)

def _gelu(x):
    return jax.nn.gelu(x, approximate=True)

def _silu(x):
    return jax.nn.silu(x)

def _sigmoid(x):
    return jax.nn.sigmoid(x)

def _layernorm(x, axis=-1, eps=1e-05):
    m = jnp.mean(x, axis=axis, keepdims=True)
    v = jnp.var(x, axis=axis, keepdims=True)
    return (x - m) / jnp.sqrt(v + eps)

def _scatter_add(tgt, idx, src, axis=0):
    return tgt.at[idx].add(src)

def _segment_sum(src, seg, n):
    return jax.ops.segment_sum(src, seg, n)
kernel_name = 'mk_gnn_resnorm_d4_gnn_r32_65c6c1'

def setup_inputs(seed: int=0):
    np.random.seed(seed)
    _w = jnp.asarray

    def _rec_inputs():
        import jax
        import jax.numpy as jnp
        _gk = jax.random.key(seed)
        x = -0.0003713 + 1 * jax.random.normal(jax.random.fold_in(_gk, 1), (3125, 128), jnp.float32)
        _s = jax.random.randint(jax.random.fold_in(_gk, 2), (25000,), 0, 3125, jnp.int32)
        _d = jax.random.randint(jax.random.fold_in(_gk, 3), (25000,), 0, 3125, jnp.int32)
        _loop = jnp.arange(3125, dtype=jnp.int32)
        src = jnp.concatenate([_s, _d, _loop])
        dst = jnp.concatenate([_d, _s, _loop])
        _o = jnp.argsort(dst, stable=True)
        src = src[_o]
        dst = dst[_o]
        edge_attr_9 = 0.000458729 + 1.00015 * jax.random.normal(jax.random.fold_in(_gk, 12), (53125, 9), jnp.float32)
        edge_weight = jax.random.uniform(jax.random.fold_in(_gk, 14), (53125,), jnp.float32, 0.0, 0.999999)
        return (x, src, dst, edge_attr_9, edge_weight)
    x, src, dst, edge_attr_9, edge_weight = _rec_inputs()

    def _L0_gnn_setup():
        import jax, jax.numpy as jnp
        import numpy as np
        N = 3125
        E = 50000
        IN = 128
        H = 128
        NH = 8
        DH = H // NH

        def _linear_init(key, fan_in, fan_out):
            kw, kb = jax.random.split(key)
            s = 1.0 / np.sqrt(fan_in)
            W = jax.random.uniform(kw, (fan_in, fan_out), jnp.float32, -s, s)
            b = jax.random.uniform(kb, (fan_out,), jnp.float32, -s, s)
            return (W, b)
        key = jax.random.key(seed)
        kx, kr, kc, k0, k1, k2, k3 = jax.random.split(key, 7)
        W_in, b_in = _linear_init(k0, IN, H)
        Wq, bq = _linear_init(k1, H, H)
        Wk, bk = _linear_init(k2, H, H)
        Wv, bv = _linear_init(k3, H, H)
        return {'X': jax.random.normal(kx, (N, IN), jnp.float32), 'rows': jax.random.randint(kr, (E,), 0, N, jnp.int32), 'cols': jax.random.randint(kc, (E,), 0, N, jnp.int32), 'W_in': W_in, 'b_in': b_in, 'Wq': Wq, 'bq': bq, 'Wk': Wk, 'bk': bk, 'Wv': Wv, 'bv': bv}
    _L0_gnn_all = _L0_gnn_setup()
    _L0_gnn_in = {k: v for k, v in _L0_gnn_all.items() if k in ('W_in', 'b_in', 'Wq', 'bq', 'Wk', 'bk', 'Wv', 'bv')}
    del _L0_gnn_all

    def _L1_gnn_setup():
        import jax, jax.numpy as jnp
        import numpy as np
        N_NODES = 3125
        N_EDGES = 50000
        D_FEAT = 128
        ALPHA = 0.1
        K_STEPS = 10

        def _spmm(edge_index, edge_vals, h, n_nodes):
            row, col = (edge_index[0], edge_index[1])
            msgs = edge_vals[:, None] * h[col]
            return jax.ops.segment_sum(msgs, row, num_segments=n_nodes)
        key = jax.random.key(seed)
        k1, k2, k3 = jax.random.split(key, 3)
        x = jax.random.normal(k1, (N_NODES, D_FEAT), dtype=jnp.float32)
        edge_index = jax.random.randint(k2, (2, N_EDGES), 0, N_NODES, dtype=jnp.int64)
        edge_vals = jax.random.uniform(k3, (N_EDGES,), dtype=jnp.float32)
        return {'x': x, 'edge_index': edge_index, 'edge_vals': edge_vals}
    _L1_gnn_all = _L1_gnn_setup()
    _L1_gnn_in = {k: v for k, v in _L1_gnn_all.items() if k in ()}
    del _L1_gnn_all

    def _L2_gnn_setup():
        import jax, jax.numpy as jnp
        import numpy as np
        N = 3125
        E = 50000
        IN = 128
        H = 4
        C = 32
        HC = H * C
        NEG_SLOPE = 0.2
        LN_EPS = 1e-05
        key = jax.random.key(seed)
        ks = jax.random.split(key, 8)
        x = jax.random.normal(ks[0], (N, IN), dtype=jnp.float32)
        edge_index = jax.random.randint(ks[1], (2, E), 0, N, dtype=jnp.int64)
        edge_weight = jax.random.uniform(ks[2], (E,), dtype=jnp.float32)
        W = jax.random.normal(ks[3], (IN, HC), dtype=jnp.float32) * (1.0 / np.sqrt(IN))
        att_src = jax.random.normal(ks[4], (H, C), dtype=jnp.float32) * (1.0 / np.sqrt(C))
        att_dst = jax.random.normal(ks[5], (H, C), dtype=jnp.float32) * (1.0 / np.sqrt(C))
        bias = jnp.zeros((HC,), dtype=jnp.float32)
        gamma = jnp.ones((HC,), dtype=jnp.float32)
        beta = jnp.zeros((HC,), dtype=jnp.float32)
        return {'x': x, 'edge_index': edge_index, 'edge_weight': edge_weight, 'W': W, 'att_src': att_src, 'att_dst': att_dst, 'bias': bias, 'gamma': gamma, 'beta': beta}
    _L2_gnn_all = _L2_gnn_setup()
    _L2_gnn_in = {k: v for k, v in _L2_gnn_all.items() if k in ('W', 'att_src', 'att_dst', 'bias', 'gamma', 'beta')}
    del _L2_gnn_all

    def _L3_gnn_setup():
        import jax, jax.numpy as jnp
        import numpy as np
        from fractions import Fraction
        from math import factorial

        def _su2_cg_coeff(j1, m1, j2, m2, j3, m3):
            if m3 != m1 + m2:
                return 0.0
            vmin = int(max(-j1 + j2 + m3, -j1 + m1, 0))
            vmax = int(min(j2 + j3 + m1, j3 - j1 + j2, j3 + m3))
            f = lambda n: factorial(round(n))
            C = ((2.0 * j3 + 1.0) * Fraction(f(j3 + j1 - j2) * f(j3 - j1 + j2) * f(j1 + j2 - j3) * f(j3 + m3) * f(j3 - m3), f(j1 + j2 + j3 + 1) * f(j1 - m1) * f(j1 + m1) * f(j2 - m2) * f(j2 + m2))) ** 0.5
            S = 0
            for v in range(vmin, vmax + 1):
                S += (-1) ** (v + j2 + m2) * Fraction(f(j2 + j3 + m1 - v) * f(j1 - m1 + v), f(v) * f(j3 - j1 + j2 - v) * f(j3 + m3 - v) * f(v + j1 - j2 - m3))
            return float(C * S)

        def _change_basis_real_to_complex(l):
            q = np.zeros((2 * l + 1, 2 * l + 1), dtype=np.complex128)
            for m in range(-l, 0):
                q[l + m, l + abs(m)] = 1 / np.sqrt(2)
                q[l + m, l - abs(m)] = -1j / np.sqrt(2)
            q[l, l] = 1
            for m in range(1, l + 1):
                q[l + m, l + abs(m)] = (-1) ** m / np.sqrt(2)
                q[l + m, l - abs(m)] = 1j * (-1) ** m / np.sqrt(2)
            return (-1j) ** l * q

        def wigner_3j(l1, l2, l3):
            C = np.zeros((2 * l1 + 1, 2 * l2 + 1, 2 * l3 + 1))
            for m1 in range(-l1, l1 + 1):
                for m2 in range(-l2, l2 + 1):
                    m3 = m1 + m2
                    if abs(m3) <= l3:
                        C[l1 + m1, l2 + m2, l3 + m3] = _su2_cg_coeff(l1, m1, l2, m2, l3, m3)
            Q1 = _change_basis_real_to_complex(l1)
            Q2 = _change_basis_real_to_complex(l2)
            Q3 = _change_basis_real_to_complex(l3)
            Cc = np.einsum('ij,kl,mn,ikn->jlm', Q1, Q2, np.conj(Q3.T), C.astype(np.complex128))
            Cr = np.real(Cc)
            return Cr / np.linalg.norm(Cr)
        MUL = 32
        IRREPS_IN = [(MUL, 0, 1), (MUL, 1, -1)]
        IRREPS_SH = [(1, 0, 1), (1, 1, -1), (1, 2, 1)]
        IRREPS_OUT = [(MUL, 0, 1), (MUL, 1, -1)]
        NUM_NEIGHBORS = 10.0
        N_NODES, N_EDGES = (10000, 3125)

        def _dim(irreps):
            return sum((m * (2 * l + 1) for m, l, _ in irreps))

        def _slices(irreps):
            s, out = (0, [])
            for m, l, _ in irreps:
                d = m * (2 * l + 1)
                out.append((s, s + d))
                s += d
            return out

        def _instructions():
            ins = []
            for i1, (m1, l1, p1) in enumerate(IRREPS_IN):
                for i2, (m2, l2, p2) in enumerate(IRREPS_SH):
                    for io, (mo, lo, po) in enumerate(IRREPS_OUT):
                        if abs(l1 - l2) <= lo <= l1 + l2 and p1 * p2 == po:
                            ins.append((i1, i2, io))
            return ins
        _INSTR = _instructions()
        _SL_IN, _SL_SH, _SL_OUT = (_slices(IRREPS_IN), _slices(IRREPS_SH), _slices(IRREPS_OUT))
        _W3J = [jnp.asarray(wigner_3j(IRREPS_IN[i1][1], IRREPS_SH[i2][1], IRREPS_OUT[io][1]), dtype=jnp.float32) for i1, i2, io in _INSTR]
        _NORM = []
        for _i1, _i2, _io in _INSTR:
            _alpha = 2 * IRREPS_OUT[_io][1] + 1
            _x = sum((IRREPS_IN[j1][0] * IRREPS_SH[j2][0] for j1, j2, jo in _INSTR if jo == _io))
            _NORM.append(float(np.sqrt(_alpha / _x)))

        def _tensor_product(x1, x2, weights):
            E = x1.shape[0]
            out = jnp.zeros((E, _dim(IRREPS_OUT)), dtype=x1.dtype)
            for k, (i1, i2, io) in enumerate(_INSTR):
                m1, l1, _ = IRREPS_IN[i1]
                m2, l2, _ = IRREPS_SH[i2]
                mo, lo, _ = IRREPS_OUT[io]
                a, b = _SL_IN[i1]
                c, d = _SL_SH[i2]
                e, f = _SL_OUT[io]
                x1s = x1[:, a:b].reshape(E, m1, 2 * l1 + 1)
                x2s = x2[:, c:d].reshape(E, m2, 2 * l2 + 1)
                seg = jnp.einsum('uvw,ijk,eui,evj->ewk', weights[k], _W3J[k], x1s, x2s, optimize='optimal') * _NORM[k]
                out = out.at[:, e:f].add(seg.reshape(E, mo * (2 * lo + 1)))
            return out
        key = jax.random.key(seed)
        ks = jax.random.split(key, 8)
        x = jax.random.normal(ks[0], (N_NODES, _dim(IRREPS_IN)), dtype=jnp.float32)
        edge_index = jax.random.randint(ks[1], (2, N_EDGES), 0, N_NODES)
        edge_attr = jax.random.normal(ks[2], (N_EDGES, _dim(IRREPS_SH)), dtype=jnp.float32)
        ws = {f'w{k}': jax.random.normal(ks[3 + k], (MUL, 1, MUL), dtype=jnp.float32) for k in range(len(_INSTR))}
        return {'x': x, 'edge_index': edge_index, 'edge_attr': edge_attr, **ws}
    _L3_gnn_all = _L3_gnn_setup()
    _L3_gnn_in = {k: v for k, v in _L3_gnn_all.items() if k in ('w0', 'w1', 'w2', 'w3', 'w4')}
    del _L3_gnn_all
    return {'x': x, 'src': src, 'dst': dst, 'edge_attr_9': edge_attr_9, 'edge_weight': edge_weight, 'L0_gnn_W_in': _L0_gnn_in['W_in'], 'L0_gnn_b_in': _L0_gnn_in['b_in'], 'L0_gnn_Wq': _L0_gnn_in['Wq'], 'L0_gnn_bq': _L0_gnn_in['bq'], 'L0_gnn_Wk': _L0_gnn_in['Wk'], 'L0_gnn_bk': _L0_gnn_in['bk'], 'L0_gnn_Wv': _L0_gnn_in['Wv'], 'L0_gnn_bv': _L0_gnn_in['bv'], 'L2_gnn_W': _L2_gnn_in['W'], 'L2_gnn_att_src': _L2_gnn_in['att_src'], 'L2_gnn_att_dst': _L2_gnn_in['att_dst'], 'L2_gnn_bias': _L2_gnn_in['bias'], 'L2_gnn_gamma': _L2_gnn_in['gamma'], 'L2_gnn_beta': _L2_gnn_in['beta'], 'L3_gnn_w0': _L3_gnn_in['w0'], 'L3_gnn_w1': _L3_gnn_in['w1'], 'L3_gnn_w2': _L3_gnn_in['w2'], 'L3_gnn_w3': _L3_gnn_in['w3'], 'L3_gnn_w4': _L3_gnn_in['w4']}

def reference(x, src, dst, edge_attr_9, edge_weight, L0_gnn_W_in, L0_gnn_b_in, L0_gnn_Wq, L0_gnn_bq, L0_gnn_Wk, L0_gnn_bk, L0_gnn_Wv, L0_gnn_bv, L2_gnn_W, L2_gnn_att_src, L2_gnn_att_dst, L2_gnn_bias, L2_gnn_gamma, L2_gnn_beta, L3_gnn_w0, L3_gnn_w1, L3_gnn_w2, L3_gnn_w3, L3_gnn_w4):
    import jax
    import jax.numpy as jnp

    def _L0_gnn_ref(X, rows, cols, W_in, b_in, Wq, bq, Wk, bk, Wv, bv):
        import jax, jax.numpy as jnp
        import numpy as np
        N = 3125
        E = 50000
        IN = 128
        H = 128
        NH = 8
        DH = H // NH

        def _linear_init(key, fan_in, fan_out):
            kw, kb = jax.random.split(key)
            s = 1.0 / np.sqrt(fan_in)
            W = jax.random.uniform(kw, (fan_in, fan_out), jnp.float32, -s, s)
            b = jax.random.uniform(kb, (fan_out,), jnp.float32, -s, s)
            return (W, b)
        h = X @ W_in + b_in
        q = (h @ Wq + bq).reshape(N, DH, NH) * DH ** (-0.5)
        k = (h @ Wk + bk).reshape(N, DH, NH)
        v = (h @ Wv + bv).reshape(N, DH, NH)
        score = jnp.einsum('edh,edh->eh', q[rows], k[cols])
        m = jax.ops.segment_max(score, rows, num_segments=N)
        p = jnp.exp(score - m[rows])
        denom = jax.ops.segment_sum(p, rows, num_segments=N)
        attn = p / denom[rows]
        out = jax.ops.segment_sum(attn[:, None, :] * v[cols], rows, num_segments=N)
        return out.reshape(N, H)

    def _L1_gnn_ref(x, edge_index, edge_vals):
        import jax, jax.numpy as jnp
        import numpy as np
        N_NODES = 3125
        N_EDGES = 50000
        D_FEAT = 128
        ALPHA = 0.1
        K_STEPS = 10

        def _spmm(edge_index, edge_vals, h, n_nodes):
            row, col = (edge_index[0], edge_index[1])
            msgs = edge_vals[:, None] * h[col]
            return jax.ops.segment_sum(msgs, row, num_segments=n_nodes)

        def body(_, h):
            return (1.0 - ALPHA) * _spmm(edge_index, edge_vals, h, N_NODES) + ALPHA * x
        return jax.lax.fori_loop(0, K_STEPS, body, x)

    def _L2_gnn_ref(x, edge_index, edge_weight, W, att_src, att_dst, bias, gamma, beta):
        import jax, jax.numpy as jnp
        import numpy as np
        N = 3125
        E = 50000
        IN = 128
        H = 4
        C = 32
        HC = H * C
        NEG_SLOPE = 0.2
        LN_EPS = 1e-05
        loops = jnp.arange(N, dtype=edge_index.dtype)
        ei = jnp.concatenate([edge_index, jnp.stack([loops, loops])], axis=1)
        src, dst = (ei[0], ei[1])
        xw = (x @ W).reshape(N, H, C)
        a_src = jnp.sum(xw * att_src, axis=-1)
        a_dst = jnp.sum(xw * att_dst, axis=-1)
        e = jax.nn.leaky_relu(a_src[src] + a_dst[dst], NEG_SLOPE)
        m = jax.ops.segment_max(e, dst, num_segments=N)
        ex = jnp.exp(e - m[dst])
        denom = jax.ops.segment_sum(ex, dst, num_segments=N)
        alpha = ex / (denom[dst] + 1e-16)
        msg = alpha[:, :, None] * xw[src]
        out = jax.ops.segment_sum(msg, dst, num_segments=N)
        out = out.reshape(N, HC) + bias
        mu = jnp.mean(out, axis=-1, keepdims=True)
        var = jnp.var(out, axis=-1, keepdims=True)
        return gamma * (out - mu) / jnp.sqrt(var + LN_EPS) + beta

    def _L3_gnn_ref(x, edge_index, edge_attr, w0, w1, w2, w3, w4):
        import jax, jax.numpy as jnp
        import numpy as np
        from fractions import Fraction
        from math import factorial

        def _su2_cg_coeff(j1, m1, j2, m2, j3, m3):
            if m3 != m1 + m2:
                return 0.0
            vmin = int(max(-j1 + j2 + m3, -j1 + m1, 0))
            vmax = int(min(j2 + j3 + m1, j3 - j1 + j2, j3 + m3))
            f = lambda n: factorial(round(n))
            C = ((2.0 * j3 + 1.0) * Fraction(f(j3 + j1 - j2) * f(j3 - j1 + j2) * f(j1 + j2 - j3) * f(j3 + m3) * f(j3 - m3), f(j1 + j2 + j3 + 1) * f(j1 - m1) * f(j1 + m1) * f(j2 - m2) * f(j2 + m2))) ** 0.5
            S = 0
            for v in range(vmin, vmax + 1):
                S += (-1) ** (v + j2 + m2) * Fraction(f(j2 + j3 + m1 - v) * f(j1 - m1 + v), f(v) * f(j3 - j1 + j2 - v) * f(j3 + m3 - v) * f(v + j1 - j2 - m3))
            return float(C * S)

        def _change_basis_real_to_complex(l):
            q = np.zeros((2 * l + 1, 2 * l + 1), dtype=np.complex128)
            for m in range(-l, 0):
                q[l + m, l + abs(m)] = 1 / np.sqrt(2)
                q[l + m, l - abs(m)] = -1j / np.sqrt(2)
            q[l, l] = 1
            for m in range(1, l + 1):
                q[l + m, l + abs(m)] = (-1) ** m / np.sqrt(2)
                q[l + m, l - abs(m)] = 1j * (-1) ** m / np.sqrt(2)
            return (-1j) ** l * q

        def wigner_3j(l1, l2, l3):
            C = np.zeros((2 * l1 + 1, 2 * l2 + 1, 2 * l3 + 1))
            for m1 in range(-l1, l1 + 1):
                for m2 in range(-l2, l2 + 1):
                    m3 = m1 + m2
                    if abs(m3) <= l3:
                        C[l1 + m1, l2 + m2, l3 + m3] = _su2_cg_coeff(l1, m1, l2, m2, l3, m3)
            Q1 = _change_basis_real_to_complex(l1)
            Q2 = _change_basis_real_to_complex(l2)
            Q3 = _change_basis_real_to_complex(l3)
            Cc = np.einsum('ij,kl,mn,ikn->jlm', Q1, Q2, np.conj(Q3.T), C.astype(np.complex128))
            Cr = np.real(Cc)
            return Cr / np.linalg.norm(Cr)
        MUL = 32
        IRREPS_IN = [(MUL, 0, 1), (MUL, 1, -1)]
        IRREPS_SH = [(1, 0, 1), (1, 1, -1), (1, 2, 1)]
        IRREPS_OUT = [(MUL, 0, 1), (MUL, 1, -1)]
        NUM_NEIGHBORS = 10.0
        N_NODES, N_EDGES = (10000, 3125)

        def _dim(irreps):
            return sum((m * (2 * l + 1) for m, l, _ in irreps))

        def _slices(irreps):
            s, out = (0, [])
            for m, l, _ in irreps:
                d = m * (2 * l + 1)
                out.append((s, s + d))
                s += d
            return out

        def _instructions():
            ins = []
            for i1, (m1, l1, p1) in enumerate(IRREPS_IN):
                for i2, (m2, l2, p2) in enumerate(IRREPS_SH):
                    for io, (mo, lo, po) in enumerate(IRREPS_OUT):
                        if abs(l1 - l2) <= lo <= l1 + l2 and p1 * p2 == po:
                            ins.append((i1, i2, io))
            return ins
        _INSTR = _instructions()
        _SL_IN, _SL_SH, _SL_OUT = (_slices(IRREPS_IN), _slices(IRREPS_SH), _slices(IRREPS_OUT))
        _W3J = [jnp.asarray(wigner_3j(IRREPS_IN[i1][1], IRREPS_SH[i2][1], IRREPS_OUT[io][1]), dtype=jnp.float32) for i1, i2, io in _INSTR]
        _NORM = []
        for _i1, _i2, _io in _INSTR:
            _alpha = 2 * IRREPS_OUT[_io][1] + 1
            _x = sum((IRREPS_IN[j1][0] * IRREPS_SH[j2][0] for j1, j2, jo in _INSTR if jo == _io))
            _NORM.append(float(np.sqrt(_alpha / _x)))

        def _tensor_product(x1, x2, weights):
            E = x1.shape[0]
            out = jnp.zeros((E, _dim(IRREPS_OUT)), dtype=x1.dtype)
            for k, (i1, i2, io) in enumerate(_INSTR):
                m1, l1, _ = IRREPS_IN[i1]
                m2, l2, _ = IRREPS_SH[i2]
                mo, lo, _ = IRREPS_OUT[io]
                a, b = _SL_IN[i1]
                c, d = _SL_SH[i2]
                e, f = _SL_OUT[io]
                x1s = x1[:, a:b].reshape(E, m1, 2 * l1 + 1)
                x2s = x2[:, c:d].reshape(E, m2, 2 * l2 + 1)
                seg = jnp.einsum('uvw,ijk,eui,evj->ewk', weights[k], _W3J[k], x1s, x2s, optimize='optimal') * _NORM[k]
                out = out.at[:, e:f].add(seg.reshape(E, mo * (2 * lo + 1)))
            return out
        i, j = (edge_index[0], edge_index[1])
        summand = _tensor_product(x[i], edge_attr, [w0, w1, w2, w3, w4])
        out = jax.ops.segment_sum(summand, j, num_segments=x.shape[0])
        return out / float(np.sqrt(NUM_NEIGHBORS))
    edge_index = jnp.stack([src, dst])
    x = _layernorm(x + _L0_gnn_ref(x, src, dst, L0_gnn_W_in, L0_gnn_b_in, L0_gnn_Wq, L0_gnn_bq, L0_gnn_Wk, L0_gnn_bk, L0_gnn_Wv, L0_gnn_bv), axis=-1)
    x = _layernorm(x + _L1_gnn_ref(x, edge_index, edge_weight), axis=-1)
    x = _layernorm(x + _L2_gnn_ref(x, edge_index, edge_weight, L2_gnn_W, L2_gnn_att_src, L2_gnn_att_dst, L2_gnn_bias, L2_gnn_gamma, L2_gnn_beta), axis=-1)
    x = _layernorm(x + _L3_gnn_ref(x, edge_index, edge_attr_9, L3_gnn_w0, L3_gnn_w1, L3_gnn_w2, L3_gnn_w3, L3_gnn_w4), axis=-1)
    return x

_drawn_inputs = setup_inputs


def setup_inputs(seed=0):
    import zlib

    import numpy as np

    out = dict(_drawn_inputs(seed))
    spreads = {'L2_gnn_bias': (0.0, 0.1), 'L2_gnn_gamma': (1.0, 0.2), 'L2_gnn_beta': (0.0, 0.1)}
    factors = {'L0_gnn_Wq': 8.0,
     'L0_gnn_bq': 5.256,
     'L0_gnn_Wk': 5.249,
     'L0_gnn_bk': 8.0,
     'L2_gnn_att_src': 8.0,
     'L2_gnn_att_dst': 8.0}
    for name, (base, spread) in spreads.items():
        noise = np.random.default_rng([zlib.crc32(name.encode()), seed]).standard_normal(out[name].shape)
        drawn = base * np.exp(spread * noise) if base else spread * noise
        out[name] = jnp.asarray(drawn.astype(out[name].dtype))
    for name, factor in factors.items():
        out[name] = (out[name] * factor).astype(out[name].dtype)
    return out
```

```python
import numpy as np
import concourse.bass as bass
from concourse import mybir
from contextlib import ExitStack

F32 = mybir.dt.float32
I32 = mybir.dt.int32
ALU = mybir.AluOpType
ACT = mybir.ActivationFunctionType
AX = mybir.AxisListType.X

P = 128
N = 3125
E = 53125
D = 128
G = 4
GE = G * P
NG = 2 * -(-E // (2 * GE))
EP = NG * GE
TN = -(-N // P)
NC = TN * P
TW = TN + 1
NP = TW * P
PAD_DST = NC - 1
MASK = 1.0e30
TRASH = NC * NC
EPS = 1.0e-5
STEPS = 10
ALPHA = 0.1


class Stage:

    def __init__(self, nc, name):
        self.nc, self.name, self.stack = nc, name, ExitStack()

    def __enter__(self):
        return self

    def __exit__(self, *error):
        return self.stack.__exit__(*error)

    def sb(self, name, shape, dtype=F32):
        return self.stack.enter_context(self.nc.sbuf_tensor(f"{self.name}_{name}", shape, dtype))

    def ps(self, name, shape):
        size = int(np.prod(shape[1:]))
        bank = self.stack.enter_context(self.nc.psum_tensor(f"{self.name}_{name}", [P, -(-size // 512) * 512], F32))
        dims = " ".join(f"d{k}" for k in range(1, len(shape)))
        sizes = {f"d{k}": shape[k] for k in range(2, len(shape))}
        return bank[0:shape[0], 0:size].rearrange(f"p ({dims}) -> p {dims}", **sizes)

    def sem(self, name):
        return self.stack.enter_context(self.nc.semaphore(f"{self.name}_{name}"))

    def block(self):
        return self.stack.enter_context(self.nc.Block())


def bc(ap, axis, n):
    shape = list(ap.shape)
    return ap.unsqueeze(axis).to_broadcast(shape[:axis] + [n] + shape[axis:])


def prepare(nc, d, c):
    with Stage(nc, "prep") as s:
        zeros = s.sb("zeros", [P, NC])
        cur = s.sb("cur", [P, EP // P], I32)
        prv = s.sb("prv", [P, EP // P], I32)
        src = s.sb("src", [P, EP // P], I32)
        brk = s.sb("brk", [P, EP // P])
        key = s.sb("key", [P, EP // P])
        end = s.sb("end", [1, 1])
        iota_i = s.sb("iota_i", [P, P], I32)
        pid_i = s.sb("pid_i", [P, 1], I32)
        loaded, zeroed, made, iotas, ones, moved, brk_ready, key_ready, stored = (
            s.sem(n) for n in ("loaded", "zeroed", "made", "iotas", "ones", "moved", "brk_ready", "key_ready",
                               "stored"))
        block = s.block()

        @block.sync
        def _(sp):
            sp.dma_start(cur[:], d.dst[1:EP + 1].rearrange("(p c) -> p c", p=P)).then_inc(loaded, 16)
            sp.dma_start(prv[:], d.dst[0:EP].rearrange("(p c) -> p c", p=P)).then_inc(loaded, 16)
            sp.dma_start(src[:], d.src.rearrange("(p c) -> p c", p=P)).then_inc(loaded, 16)
            sp.dma_start(c.bases[:], d.bases).then_inc(loaded, 16)
            sp.dma_start(c.x[:], d.x.rearrange("(t p) f -> p t f", p=P)).then_inc(loaded, 16)
            sp.wait_ge(zeroed, 2)
            for t in range(TN):
                rows = d.A[t * P * NC:(t + 1) * P * NC].rearrange("(p r) -> p r", p=P)
                sp.dma_start(rows, zeros[:]).then_inc(stored, 16)
            sp.dma_start(d.A[TRASH:TRASH + P].rearrange("(p r) -> p r", p=P), zeros[:, 0:1]).then_inc(stored, 16)
            sp.dma_start(d.brk[EP:EP + 1].rearrange("(p r) -> p r", p=1), end[:]).then_inc(stored, 16)
            sp.wait_ge(brk_ready, 1)
            sp.dma_start(d.brk[0:EP].rearrange("(p c) -> p c", p=P), brk[:]).then_inc(stored, 16)
            sp.wait_ge(key_ready, 1)
            sp.dma_start(d.key.rearrange("(p c) -> p c", p=P), key[:]).then_inc(stored, 16)
            sp.wait_ge(loaded, 80)
            sp.wait_ge(stored, 16 * (TN + 4))

        @block.gpsimd
        def _(pool):
            nc.gpsimd.memset(c.ident[:], 1.0).then_inc(ones, 1)
            nc.gpsimd.memset(c.lower[:], 1.0).then_inc(ones, 1)
            nc.gpsimd.iota(iota_i[:], pattern=[[1, P]], base=0, channel_multiplier=0).then_inc(iotas, 1)
            nc.gpsimd.iota(pid_i[:], pattern=[[0, 1]], base=0, channel_multiplier=1).then_inc(iotas, 1)
            pool.wait_ge(ones, 2)
            nc.gpsimd.affine_select(out=c.ident[:], in_=c.ident[:], compare_op=ALU.is_equal, fill=0.0,
                                    base=0, pattern=[[-1, P]], channel_multiplier=1).then_inc(made, 1)
            nc.gpsimd.affine_select(out=c.lower[:], in_=c.lower[:], compare_op=ALU.is_gt, fill=0.0,
                                    base=0, pattern=[[-1, P]], channel_multiplier=1).then_inc(made, 1)
            pool.wait_ge(made, 2)

        @block.vector
        def _(dve):
            nc.vector.memset(zeros[:], 0.0).then_inc(zeroed, 1)
            nc.vector.memset(end[:], -MASK).then_inc(zeroed, 1)
            dve.wait_ge(iotas, 2)
            nc.vector.tensor_copy(c.iota[:], iota_i[:]).then_inc(moved, 1)
            nc.vector.tensor_copy(c.pid[:], pid_i[:]).then_inc(moved, 1)
            dve.wait_ge(loaded, 80)
            nc.vector.tensor_tensor(brk[:], prv[:], cur[:], ALU.subtract).then_inc(moved, 1)
            dve.wait_ge(moved, 3)
            nc.vector.tensor_scalar(c.trash[:], c.pid[:], float(TRASH), None, ALU.add).then_inc(moved, 1)
            nc.vector.tensor_scalar(brk[:], brk[:], MASK, None, ALU.mult).then_inc(brk_ready, 1)
            nc.vector.scalar_tensor_tensor(key[:], cur[:], float(NC), src[:], ALU.mult,
                                           ALU.add).then_inc(key_ready, 1)
            dve.wait_ge(moved, 4)


def node_tables(nc, c, s, loads, fix, w_row, stores, hidden=None, b_row=None):
    width = w_row.shape[1]
    xs = [s.sb(f"xs{b}", [P, P]) for b in range(2)]
    xt = [s.sb(f"xt{b}", [P, P]) for b in range(2)]
    ht = [s.sb(f"ht{b}", [P, P]) for b in range(2)]
    rows = [s.sb(f"rows{b}", [P, width]) for b in range(2)]
    p_xt = [s.ps(f"p_xt{b}", [P, P]) for b in range(2)]
    p_ht = [s.ps(f"p_ht{b}", [P, P]) for b in range(2)]
    p_rows = [s.ps(f"p_rows{b}", [P, width]) for b in range(2)]
    loaded, cleared, weights, chained, staged, transposed, xt_ready, hid, ht_ready, multiplied, rows_ready = (
        s.sem(n) for n in ("loaded", "cleared", "weights", "chained", "staged", "transposed", "xt_ready", "hid",
                           "ht_ready", "multiplied", "rows_ready"))
    stored = [s.sem(f"stored{b}") for b in range(2)]
    block = s.block()

    @block.sync
    def _(sp):
        sp.wait_ge(cleared, 1)
        for tile, source in loads:
            sp.dma_start(tile, source).then_inc(loaded, 16)
        with sp.Fori(0, TW // 2) as i:
            for b in range(2):
                sp.wait_ge(rows_ready, i * 2 + (b + 1))
                for table, a, z in stores:
                    sp.dma_start(table[bass.ds((i * 2 + b) * P, P), :], rows[b][:, a:z]).then_inc(stored[b], 16)
        for b in range(2):
            sp.wait_ge(stored[b], 16 * len(stores) * (TW // 2 + 1))

    @block.vector
    def _(dve):
        count = [0]

        def chain(instruction):
            count[0] += 1
            instruction.then_inc(chained, 1)
            dve.wait_ge(chained, count[0])

        fix.clear(chain)
        dve.sem_inc(cleared, 1)
        dve.wait_ge(loaded, 16 * len(loads))
        fix.finish(chain)
        dve.sem_inc(weights, 1)
        for b in range(2):
            dve.sem_inc(stored[b], 16 * len(stores))
        with dve.Fori(0, TW // 2) as i:
            for b in range(2):
                t = i * 2 + b
                dve.wait_ge(transposed, t + 1)
                nc.vector.tensor_copy(xs[b][:], c.x[:, bass.ds(t, 1), :]).then_inc(staged, 1)
                dve.wait_ge(multiplied, t + 1)
                dve.wait_ge(stored[b], (i + 1) * (16 * len(stores)))
                if b_row is None:
                    nc.vector.tensor_copy(rows[b][:], p_rows[b][:]).then_inc(rows_ready, 1)
                else:
                    nc.vector.tensor_tensor(rows[b][:], p_rows[b][:], b_row[:], ALU.add).then_inc(rows_ready, 1)

    @block.scalar
    def _(act):
        act.wait_ge(weights, 1)
        with act.Fori(0, TW // 2) as i:
            for b in range(2):
                act.wait_ge(transposed, i * 2 + (b + 2))
                nc.scalar.copy(xt[b][:], p_xt[b][:]).then_inc(xt_ready, 1)
                if hidden:
                    act.wait_ge(hid, i * 2 + (b + 1))
                    nc.scalar.activation(ht[b][:], p_ht[b][:], ACT.Identity, bias=hidden[1][:]).then_inc(ht_ready, 1)

    @block.tensor
    def _(pe):
        pe.wait_ge(weights, 1)
        pe.sem_inc(transposed, 1)
        with pe.Fori(0, TW // 2) as i:
            for b in range(2):
                t = i * 2 + b
                pe.wait_ge(staged, t + 1)
                nc.tensor.transpose(p_xt[b][:], xs[b][:], c.ident[:]).then_inc(transposed, 1)
                pe.wait_ge(xt_ready, t + 1)
                if hidden:
                    nc.tensor.matmul(p_ht[b][:], hidden[0][:], xt[b][:], start=True, stop=True).then_inc(hid, 1)
                    pe.wait_ge(ht_ready, t + 1)
                nc.tensor.matmul(p_rows[b][:], (ht if hidden else xt)[b][:], w_row[:], start=True,
                                 stop=True).then_inc(multiplied, 1)


class Fix:

    def __init__(self, clear, finish):
        self.clear, self.finish = clear, finish


def attention_tables(nc, d, c):
    with Stage(nc, "qkv") as s:
        w_in = s.sb("w_in", [P, D])
        b_in = s.sb("b_in", [P, 1])
        w_qkv = s.sb("w_qkv", [P, 3 * D])
        b_qkv = s.sb("b_qkv", [P, 3 * D])
        loads = [(w_in[:], d.W_in), (b_in[:], d.b_in.rearrange("(p o) -> p o", o=1))]
        for n, (w, b) in enumerate(((d.Wq, d.bq), (d.Wk, d.bk), (d.Wv, d.bv))):
            loads += [(w_qkv[:, n * D:(n + 1) * D], w), (b_qkv[:, n * D:(n + 1) * D], bc(b, 0, P))]

        def finish(chain):
            chain(nc.vector.tensor_scalar(w_qkv[:, 0:D], w_qkv[:, 0:D], 0.25, None, ALU.mult))
            chain(nc.vector.tensor_scalar(b_qkv[:, 0:D], b_qkv[:, 0:D], 0.25, None, ALU.mult))

        node_tables(nc, c, s, loads, Fix(lambda chain: None, finish), w_qkv,
                    [(d.q_rows, 0, D), (d.kv_rows, D, 3 * D)], (w_in, b_in), b_qkv)


def gat_tables(nc, d, c):
    H, HD = 4, 32
    with Stage(nc, "gatw") as s:
        w = s.sb("w", [P, D])
        b0 = s.sb("b0", [P, 1])
        heads = s.sb("heads", [P, D + 2 * H])
        loads = [(w[:], d.W2)]
        for n, att in enumerate((d.att_src, d.att_dst)):
            for h in range(H):
                col = D + n * H + h
                loads.append((heads[h * HD:(h + 1) * HD, col:col + 1], att[h, :].rearrange("(p o) -> p o", o=1)))

        def clear(chain):
            chain(nc.vector.memset(b0[:], 0.0))
            chain(nc.vector.tensor_copy(heads[:, 0:D], c.ident[:]))
            chain(nc.vector.memset(heads[:, D:], 0.0))

        node_tables(nc, c, s, loads, Fix(clear, lambda chain: None), heads,
                    [(d.xw_rows, 0, D + H), (d.dst_rows, D + H, D + 2 * H)], (w, b0))


U = 32
TPW = D + 7 * U


def tensor_tables(nc, d, c):
    C0, C1 = (1 / 64) ** 0.5 / 10 ** 0.5, (3 / 96) ** 0.5 / 10 ** 0.5
    third = 3 ** -0.5
    scale = [C0, C1 * third, C1 * third, C0 * third, C1]
    with Stage(nc, "tpw") as s:
        w = s.sb("w", [P, TPW])
        v2 = s.sb("v2", [P, 3, U])
        sU, sV = w[:, D:D + U], w[:, D + U:].rearrange("p (n i w) -> p n i w", n=2, i=3)
        loads = [(w[0:U, 0:U], d.w[0]), (w[0:U, D:D + U], d.w[1])]
        for i in range(3):
            comp = slice(U + i, P, 3)
            loads += [(v2[comp, i, :], d.w[2]), (sV[comp, 0, i, :], d.w[3]), (sV[comp, 1, i, :], d.w[4])]

        def clear(chain):
            chain(nc.vector.memset(w[:], 0.0))
            chain(nc.vector.memset(v2[:], 0.0))

        def finish(chain):
            chain(nc.vector.tensor_scalar(w[:, 0:U], w[:, 0:U], scale[0], None, ALU.mult))
            chain(nc.vector.tensor_scalar(w[:, U:D].rearrange("p (w i) -> p i w", i=3), v2[:], scale[2], None,
                                          ALU.mult))
            chain(nc.vector.tensor_scalar(sU, sU, scale[1], None, ALU.mult))
            for n in range(2):
                chain(nc.vector.tensor_scalar(sV[:, n], sV[:, n], scale[3 + n], None, ALU.mult))

        node_tables(nc, c, s, loads, Fix(clear, finish), w, [(d.tp_rows, 0, TPW)])


def softmax_edges(nc, d, c, name, H, window, table, V0, acc, scatter):
    dots = H == 8
    WD, TD, HD = window.shape[1], table.shape[1], D // H
    with Stage(nc, name) as s:
        two = range(2)
        cols = [s.sb(f"cols{b}", [P, 4 * G], I32) for b in two]
        dst_row = [s.sb(f"dst_row{b}", [P, GE], I32) for b in two]
        brk_row = [s.sb(f"brk_row{b}", [H, GE + 1]) for b in two]
        win = [s.sb(f"win{b}", [P, G, WD]) for b in two]
        gat = [s.sb(f"gat{b}", [P, G, TD]) for b in two]
        off = [s.sb(f"off{b}", [P, 2, G]) for b in two]
        away = s.sb("away", [P, 2, GE])
        pick = [s.sb(f"pick{b}", [P, G, P]) for b in two]
        pick_t = [s.sb(f"pick_t{b}", [P, G, P]) for b in two]
        prod = s.sb("prod", [P, G, D])
        score = [s.sb(f"score{b}", [P, G, H]) for b in two]
        run = s.sb("run", [H, GE])
        top = [s.sb(f"top{b}", [H, GE]) for b in two]
        step_up = s.sb("step_up", [H, 1])
        decay = s.sb("decay", [H, 1])
        decay_f = s.sb("decay_f", [P, 1])
        less = s.sb("less", [P, G, H])
        prob = s.sb("prob", [P, G, D])
        count = [s.sb(f"count{b}", [P, 2, G]) for b in two]
        msg = s.sb("msg", [P, G, D])
        spread = s.sb("spread", [H, P])
        p_exp = s.ps("p_exp", [P, G, WD])
        p_score = s.ps("p_score", [H, GE])
        p_top = s.ps("p_top", [P, G, H])
        p_decay = s.ps("p_decay", [P, 1])
        p_sum = s.ps("p_sum", [P, G, 2, P])
        if scatter:
            key_row = [s.sb(f"key_row{b}", [P, GE]) for b in two]
            wcol = [s.sb(f"wcol{b}", [P, G]) for b in two]
            key = s.sb("key", [P, G])
            same = s.sb("same", [P, G, P])
            repeats = s.sb("repeats", [P, G])
            first = s.sb("first", [P, G])
            to_f = s.sb("to_f", [P, G])
            to = [s.sb(f"to{b}", [P, G], I32) for b in two]
            add = [s.sb(f"add{b}", [P, G]) for b in two]
            p_add = s.ps("p_add", [P, G])
            same_ready, added, targets, added_up = (
                s.sem(n) for n in ("same_ready", "added", "targets", "added_up"))
        ready = [s.sem(f"ready{b}") for b in two]
        gathered = [s.sem(f"gathered{b}") for b in two]
        (passed, offsets, messages, done, picked, expanded, scored, flipped, topped, lowered, exped, weighed, summed, vec, spread_ready,
         awayed) = (s.sem(n) for n in ("passed", "offsets", "messages", "done", "picked", "expanded", "scored", "flipped", "topped", "lowered",
                                       "exped", "weighed", "summed", "vec", "spread_ready", "awayed"))
        LOADS = (3 + G + (2 if scatter else 0)) * 16
        VEC = 3 + G + (1 if dots else 5) + (G + 4 if scatter else 0)
        pattern = "p t (d h) -> p t d h" if dots else "p t (h d) -> p t h d"
        block = s.block()

        @block.sync
        def _(sp):
            with sp.Fori(0, NG // 2) as i:
                for b in two:
                    g = i * 2 + b
                    sp.wait_ge(done, g + 1)
                    sp.dma_start(cols[b][:], d.cols[bass.ds(g, 1), :, :]).then_inc(ready[b], 16)
                    sp.dma_start(dst_row[b][:], bc(d.dst[bass.ds(g * GE + 1, GE)], 0, P)).then_inc(ready[b], 16)
                    sp.dma_start(brk_row[b][:], bc(d.brk[bass.ds(g * GE, GE + 1)], 0, H)).then_inc(ready[b], 16)
                    if scatter:
                        sp.dma_start(key_row[b][:], bc(d.key[bass.ds(g * GE, GE)], 0, P)).then_inc(ready[b], 16)
                        sp.dma_start(wcol[b][:], d.wcol[bass.ds(g, 1), :, :]).then_inc(ready[b], 16)
                    for t in range(G):
                        base = sp.value_load(c.bases[0:1, bass.ds(g * G + t, 1)], min_val=0, max_val=NC - 1)
                        sp.dma_start(win[b][:, t, :], window[bass.ds(base, P), :]).then_inc(ready[b], 16)

        @block.gpsimd
        def _(pool):
            with pool.Fori(0, NG // 2) as i:
                for b in two:
                    g = i * 2 + b
                    pool.wait_ge(ready[b], (i + 1) * LOADS)
                    pool.sem_inc(passed, 1)
                    for t in range(G):
                        pool.indirect_dma_start(
                            gat[b][:, t, :], None, table,
                            bass.IndirectOffsetOnAxis(ap=cols[b][:, t:t + 1], axis=0)).then_inc(gathered[b], 16)
                    if scatter:
                        pool.wait_ge(targets, (g + 1) * 2)
                        pool.sem_inc(passed, 1)
                        for t in range(G):
                            pool.indirect_dma_start(
                                d.A.rearrange("(n o) -> n o", o=1),
                                bass.IndirectOffsetOnAxis(ap=to[b][:, t:t + 1], axis=0),
                                add[b][:, t:t + 1], None, compute_op=ALU.add).then_inc(added_up, 16)
                            pool.wait_ge(added_up, (g * G + (t + 1)) * 16)
                            pool.sem_inc(passed, 1)

        @block.scalar
        def _(act):
            with act.Fori(0, NG // 2) as i:
                for b in two:
                    g = i * 2 + b
                    act.wait_ge(offsets, (g + 1) * 2)
                    act.wait_ge(ready[b], (i + 1) * LOADS)
                    for t in range(G):
                        nc.scalar.activation(away[:, 0, t * P:(t + 1) * P], dst_row[b][:, t * P:(t + 1) * P], ACT.Abs,
                                             bias=off[b][:, 1, t:t + 1]).then_inc(awayed, 1)
                        nc.scalar.activation(away[:, 1, t * P:(t + 1) * P], c.iota[:], ACT.Abs,
                                             bias=off[b][:, 0, t:t + 1]).then_inc(awayed, 1)
                    act.wait_ge(awayed, (g + 1) * 2 * G)
                    nc.scalar.activation(pick_t[b][:], away[:, 0, :].rearrange("p (t e) -> p t e", t=G), ACT.Relu,
                                         scale=-1.0, bias=1.0).then_inc(picked, 1)
                    if dots:
                        nc.scalar.activation(pick[b][:], away[:, 1, :].rearrange("p (t e) -> p t e", t=G), ACT.Relu,
                                             scale=-1.0, bias=1.0).then_inc(picked, 1)
                    else:
                        for t in range(G):
                            last = nc.scalar.activation(pick[b][:, t, :], away[:, 1, t * P:(t + 1) * P], ACT.Relu,
                                                        scale=count[b][:, 1, t:t + 1], bias=count[b][:, 0, t:t + 1])
                        last.then_inc(picked, 1)
                    act.wait_ge(picked, (g + 1) * 2)
                    act.wait_ge(topped, g + 1)
                    nc.scalar.activation(decay[:], step_up[:], ACT.Exp, scale=-1.0).then_inc(exped, 1)
                    act.wait_ge(lowered, g + 1)
                    nc.scalar.activation(
                        prob[:].rearrange(pattern, h=H), bc(less[:], 2, HD) if dots else bc(less[:], 3, HD),
                        ACT.Exp).then_inc(exped, 1)

        @block.vector
        def _(dve):
            dve.sem_inc(done, 2)
            heads = c.ident[0:H, 0:H]
            if dots:
                view, like = spread[:].rearrange("h (d k) -> h d k", k=H), bc(heads, 1, HD)
            else:
                view, like = spread[:].rearrange("h (k d) -> h k d", k=H), bc(heads, 2, HD)
            nc.vector.tensor_copy(view, like).then_inc(spread_ready, 1)
            nc.vector.memset(top[1][:], -MASK).then_inc(spread_ready, 1)
            nc.vector.memset(acc[:], 0.0).then_inc(spread_ready, 1)
            dve.wait_ge(spread_ready, 3)
            with dve.Fori(0, NG // 2) as i:
                for b in two:
                    g = i * 2 + b
                    n = [0]

                    def step(instruction, wait=True):
                        n[0] += 1
                        instruction.then_inc(vec, 1)
                        if wait:
                            dve.wait_ge(vec, g * VEC + n[0])

                    src, dst, base, after = (cols[b][:, k * G:(k + 1) * G] for k in range(4))
                    dve.wait_ge(ready[b], (i + 1) * LOADS)
                    if not dots:
                        step(nc.vector.tensor_tensor(count[b][:, 1, :], after, dst, ALU.not_equal))
                        step(nc.vector.tensor_scalar(count[b][:, 0, :], count[b][:, 1, :], 1.0, None, ALU.add))
                        step(nc.vector.tensor_scalar(count[b][:, 1, :], count[b][:, 0, :], -1.0, None, ALU.mult))
                    nc.vector.tensor_tensor(off[b][:, 0, :], base, dst, ALU.subtract).then_inc(offsets, 1)
                    nc.vector.tensor_scalar(off[b][:, 1, :], base, c.pid[:], -1.0, ALU.add,
                                            ALU.mult).then_inc(offsets, 1)
                    dve.wait_ge(gathered[b], (i + 1) * G * 16)
                    if scatter:
                        step(nc.vector.scalar_tensor_tensor(key[:], dst, float(NC), src, ALU.mult, ALU.add))
                        for t in range(G):
                            step(nc.vector.scalar_tensor_tensor(
                                same[:, t, :], key_row[b][:, t * P:(t + 1) * P], key[:, t:t + 1], c.lower[:],
                                ALU.is_equal, ALU.mult), t == G - 1)
                        nc.vector.tensor_reduce(repeats[:], same[:], AX, ALU.add).then_inc(same_ready, 1)
                        dve.wait_ge(same_ready, g + 1)
                        step(nc.vector.tensor_scalar(first[:], repeats[:], 0.0, None, ALU.is_equal), False)
                        step(nc.vector.tensor_scalar(to_f[:], key[:], c.trash[:], None, ALU.subtract))
                        step(nc.vector.tensor_tensor(to_f[:], to_f[:], first[:], ALU.mult))
                        nc.vector.tensor_scalar(to[b][:], to_f[:], c.trash[:], None, ALU.add).then_inc(targets, 1)
                        dve.wait_ge(added, g + 1)
                        nc.vector.tensor_tensor(add[b][:], p_add[:], wcol[b][:], ALU.add).then_inc(targets, 1)
                    dve.wait_ge(expanded, g + 1)
                    if dots:
                        step(nc.vector.tensor_tensor(prod[:], p_exp[:], gat[b][:, :, 0:D], ALU.mult))
                        nc.vector.tensor_reduce(score[b][:], prod[:].rearrange("p t (d h) -> p t h d", h=H), AX,
                                                ALU.add).then_inc(scored, 1)
                    else:
                        step(nc.vector.tensor_tensor(prod[:, :, 0:H], p_exp[:], gat[b][:, :, D:D + H], ALU.add))
                        step(nc.vector.tensor_scalar(prod[:, :, H:2 * H], prod[:, :, 0:H], 0.2, None, ALU.mult))
                        nc.vector.tensor_tensor(score[b][:], prod[:, :, 0:H], prod[:, :, H:2 * H],
                                                ALU.max).then_inc(scored, 1)
                    dve.wait_ge(flipped, g + 1)
                    step(nc.vector.tensor_tensor_scan(run[:], brk_row[b][:, 0:GE], p_score[:],
                                                      top[1 - b][:, GE - 1:GE], ALU.add, ALU.max))
                    step(nc.vector.tensor_tensor_scan(top[b][:, ::-1], brk_row[b][:, GE:0:-1], run[:, ::-1],
                                                      -MASK, ALU.add, ALU.max))
                    nc.vector.tensor_scalar(step_up[:], top[b][:, 0:1], top[1 - b][:, GE - 1:GE], 0.0,
                                            ALU.subtract, ALU.max).then_inc(topped, 1)
                    dve.wait_ge(weighed, 2 * g + 1)
                    nc.vector.tensor_tensor(less[:], score[b][:],
                                            p_top[:],
                                            ALU.subtract).then_inc(lowered, 1)
                    dve.wait_ge(exped, 2 * g + 2)
                    nc.vector.tensor_tensor(msg[:], gat[b][:, :, V0:V0 + D], prob[:], ALU.mult).then_inc(messages, 1)
                    dve.wait_ge(weighed, 2 * g + 2)
                    step(nc.vector.tensor_copy(decay_f[:], p_decay[:]))
                    dve.wait_ge(summed, g + 1)
                    for t in range(G):
                        base = dve.value_load(c.bases[0:1, bass.ds(g * G + t, 1)], min_val=0, max_val=NC - 1)
                        if t == 0:
                            at = acc[:, :, bass.ds(base, 1)]
                            step(nc.vector.tensor_scalar(at, at, decay_f[:], None, ALU.mult))
                        at = acc[:, :, bass.ds(base, P)]
                        instruction = nc.vector.tensor_tensor(at, at, p_sum[:, t, :, :], ALU.add)
                        if t < G - 1:
                            step(instruction)
                        else:
                            instruction.then_inc(done, 1)
                            dve.wait_ge(done, g + 3)
                    assert n[0] == VEC

        @block.tensor
        def _(pe):
            pe.wait_ge(spread_ready, 3)
            with pe.Fori(0, NG // 2) as i:
                for b in two:
                    g = i * 2 + b
                    pe.wait_ge(ready[b], (i + 1) * LOADS)
                    pe.wait_ge(picked, g * 2 + 1)
                    for t in range(G):
                        last = nc.tensor.matmul(p_exp[:, t, :], pick_t[b][:, t, :], win[b][:, t, :],
                                                start=True, stop=True)
                    last.then_inc(expanded, 1)
                    if scatter:
                        pe.wait_ge(same_ready, g + 1)
                        for t in range(G):
                            last = nc.tensor.matmul(p_add[:, t:t + 1], same[:, t, :], wcol[b][:, t:t + 1],
                                                    start=True, stop=True)
                        last.then_inc(added, 1)
                    pe.wait_ge(scored, g + 1)
                    for t in range(G):
                        last = nc.tensor.transpose(p_score[:, t * P:(t + 1) * P], score[b][:, t, :], c.ident[:])
                    last.then_inc(flipped, 1)
                    pe.wait_ge(topped, g + 1)
                    for t in range(G):
                        last = nc.tensor.matmul(p_top[:, t, :], top[b][:, t * P:(t + 1) * P], c.ident[0:H, 0:H],
                                                start=True, stop=True)
                    last.then_inc(weighed, 1)
                    pe.wait_ge(exped, 2 * g + 1)
                    nc.tensor.matmul(p_decay[:], spread[:], decay[:], start=True,
                                     stop=True).then_inc(weighed, 1)
                    pe.wait_ge(picked, g * 2 + 2)
                    pe.wait_ge(messages, g + 1)
                    for t in range(G):
                        nc.tensor.matmul(p_sum[:, t, 0, :], msg[:, t, :], pick[b][:, t, :], start=True, stop=True)
                        last = nc.tensor.matmul(p_sum[:, t, 1, :], prob[:, t, :], pick[b][:, t, :],
                                                start=True, stop=True)
                    last.then_inc(summed, 1)


def finish_layer(nc, d, c, name, divide=None, inner=None, out=None):
    with Stage(nc, name) as s:
        y = s.sb("y", [P, TN, D])
        sq = s.sb("sq", [P, TN, D])
        stats = s.sb("stats", [P, 3, TN])
        rows = s.sb("rows", [P, 3, D])
        p_t = [s.ps(f"p_t{k}", [P, 4, P]) for k in range(7)]
        loaded, chained, quotient, flipped, asked, rooted, ended, stored = (
            s.sem(n) for n in ("loaded", "chained", "quotient", "flipped", "asked", "rooted", "ended", "stored"))
        block = s.block()
        quads = [(k, min(k + 4, TN)) for k in range(0, TN, 4)]
        x = c.x[:, 0:TN, :]
        yt, den = c.acc[:, 0, 0:NC], c.acc[:, 1, 0:NC]

        @block.sync
        def _(sp):
            if inner:
                for k in range(3):
                    sp.dma_start(rows[:, k, :], bc(inner[k], 0, P)).then_inc(loaded, 16)
            if out is not None:
                sp.wait_ge(ended, 1)
                whole = N // P
                sp.dma_start(out[0:whole * P, :].rearrange("(t p) f -> p t f", p=P),
                             c.x[:, 0:whole, :]).then_inc(stored, 16)
                sp.dma_start(out[whole * P:N, :], c.x[0:N - whole * P, whole, :]).then_inc(stored, 16)
                sp.wait_ge(stored, 32)

        @block.tensor
        def _(pe):
            pe.wait_ge(quotient, 1)
            for q, (a, z) in enumerate(quads):
                for t in range(a, z):
                    last = nc.tensor.transpose(p_t[q][:, t - a, :], c.acc[:, 0, t * P:(t + 1) * P], c.ident[:])
                last.then_inc(flipped, 1)

        @block.scalar
        def _(act):
            var = stats[:, 1, :]
            for k in range(2 if inner else 1):
                act.wait_ge(asked, k + 1)
                nc.scalar.activation(stats[:, 2, :], var, ACT.Sqrt).then_inc(rooted, 1)

        @block.vector
        def _(dve):
            count = [0]

            def chain(instruction):
                count[0] += 1
                instruction.then_inc(chained, 1)
                dve.wait_ge(chained, count[0])

            norms = [0]

            def layernorm():
                mean, var, std = (stats[:, k, :] for k in range(3))
                chain(nc.vector.tensor_reduce(mean, y[:], AX, ALU.add))
                chain(nc.vector.tensor_scalar(mean, mean, 1.0 / D, None, ALU.mult))
                chain(nc.vector.tensor_tensor(y[:], y[:], bc(mean, 2, D), ALU.subtract))
                chain(nc.vector.tensor_tensor(sq[:], y[:], y[:], ALU.mult))
                chain(nc.vector.tensor_reduce(var, sq[:], AX, ALU.add))
                nc.vector.tensor_scalar(var, var, 1.0 / D, EPS, ALU.mult, ALU.add).then_inc(asked, 1)
                norms[0] += 1
                dve.wait_ge(rooted, norms[0])
                chain(nc.vector.reciprocal(std, std))
                chain(nc.vector.tensor_tensor(y[:], y[:], bc(std, 2, D), ALU.mult))

            if divide is not None:
                chain(nc.vector.tensor_scalar(den, den, divide, 1.0e-30, ALU.add, ALU.max))
                chain(nc.vector.reciprocal(den, den))
                chain(nc.vector.tensor_tensor(yt, yt, den, ALU.mult))
            dve.sem_inc(quotient, 1)
            if inner:
                dve.wait_ge(loaded, 48)
            bias, gamma, beta = (bc(rows[:, k, :], 1, TN) for k in range(3))
            for q, (a, z) in enumerate(quads):
                dve.wait_ge(flipped, q + 1)
                other = bias[:, a:z, :] if inner else x[:, a:z, :]
                chain(nc.vector.tensor_tensor(y[:, a:z, :], p_t[q][:, 0:z - a, :], other, ALU.add))
            if inner:
                layernorm()
                chain(nc.vector.tensor_tensor(y[:], y[:], gamma, ALU.mult))
                chain(nc.vector.tensor_tensor(y[:], y[:], beta, ALU.add))
                chain(nc.vector.tensor_tensor(y[:], y[:], x, ALU.add))
            layernorm()
            chain(nc.vector.tensor_copy(x, y[:]))
            dve.sem_inc(ended, 1)


def propagate(nc, d, c):
    RING, KEEP = 4, 5
    CH = 512
    chunks = [(k, min(k + CH, NC)) for k in range(0, NC, CH)]
    assert (TN - KEEP) % RING == 0
    with Stage(nc, "prop") as s:
        kept = s.sb("kept", [P, KEEP, NC])
        ring = [s.sb(f"ring{k}", [P, NC]) for k in range(RING)]
        h = s.sb("h", [P, TN, D])
        ht = c.acc[:, 0, 0:NC]
        x01 = s.sb("x01", [P, NC])
        p_h = s.ps("p_h", [P, len(chunks) * CH])
        p_t = s.ps("p_t", [P, 4, P])
        kept_in, x_flipped, x01_ready, h_ready, evacuated, block_done, flipped, started = (
            s.sem(n) for n in ("kept_in", "x_flipped", "x01_ready", "h_ready", "evacuated", "block_done",
                               "flipped", "started"))
        landed = [s.sem(f"landed{k}") for k in range(RING)]
        used = [s.sem(f"used{k}") for k in range(RING)]
        block = s.block()
        turns = (TN - KEEP) // RING
        quads = [(k, min(k + 4, TN)) for k in range(0, TN, 4)]
        A = d.A[0:NC * NC].rearrange("(k p r) -> k p r", k=TN, p=P)

        @block.sync
        def _(sp):
            for k in range(KEEP):
                sp.dma_start(kept[:, k, :], A[k]).then_inc(kept_in, 16)
            for k in range(RING):
                sp.sem_inc(used[k], 1)
            with sp.Fori(0, STEPS) as i:
                for k in range(KEEP, TN):
                    slot, turn = (k - KEEP) % RING, (k - KEEP) // RING
                    sp.wait_ge(used[slot], i * turns + (turn + 1))
                    sp.dma_start(ring[slot][:], A[k]).then_inc(landed[slot], 16)

        @block.tensor
        def _(pe):
            for q, (a, z) in enumerate(quads):
                if q:
                    pe.wait_ge(x01_ready, q)
                for t in range(a, z):
                    last = nc.tensor.transpose(p_t[:, t - a, :], c.x[:, t, :], c.ident[:])
                last.then_inc(x_flipped, 1)
            pe.wait_ge(h_ready, len(quads))
            pe.wait_ge(x01_ready, len(quads))
            pe.wait_ge(kept_in, 16 * KEEP)
            with pe.Fori(0, STEPS) as i:
                for k in range(TN):
                    if k >= KEEP:
                        slot, turn = (k - KEEP) % RING, (k - KEEP) // RING
                        pe.wait_ge(landed[slot], (i * turns + (turn + 1)) * 16)
                    rows = kept[:, k, :] if k < KEEP else ring[slot][:]
                    for n, (a, z) in enumerate(chunks):
                        last = nc.tensor.matmul(p_h[:, a:z], h[:, k, :], rows[:, a:z], start=k == 0,
                                                stop=k == TN - 1)
                        if k == TN - 1:
                            last.then_inc(block_done, 1)
                    if KEEP <= k < TN - 1:
                        last.then_inc(used[slot], 1)
                    elif k == TN - 1:
                        pe.wait_ge(block_done, (i + 1) * len(chunks))
                        pe.sem_inc(used[slot], 1)
                for q, (a, z) in enumerate(quads):
                    pe.wait_ge(evacuated, i * len(chunks) + (z * P + CH - 1) // CH)
                    pe.wait_ge(h_ready, i * len(quads) + len(quads) + q)
                    for t in range(a, z):
                        last = nc.tensor.transpose(p_t[:, t - a, :], ht[:, t * P:(t + 1) * P], c.ident[:])
                    last.then_inc(flipped, 1)
                pe.wait_ge(h_ready, i * len(quads) + 2 * len(quads))

        @block.vector
        def _(dve):
            for q, (a, z) in enumerate(quads):
                dve.wait_ge(x_flipped, q + 1)
                nc.vector.tensor_scalar(x01[:, a * P:z * P], p_t[:, 0:z - a, :].rearrange("p t n -> p (t n)"),
                                        ALPHA, None, ALU.mult).then_inc(x01_ready, 1)
            with dve.Fori(0, STEPS) as i:
                for n, (a, z) in enumerate(chunks):
                    dve.wait_ge(block_done, i * len(chunks) + (n + 1))
                    nc.vector.scalar_tensor_tensor(ht[:, a:z], p_h[:, a:z], 1.0 - ALPHA, x01[:, a:z], ALU.mult,
                                                   ALU.add).then_inc(evacuated, 1)

        @block.scalar
        def _(act):
            for a, z in quads:
                nc.scalar.copy(h[:, a:z, :], c.x[:, a:z, :]).then_inc(h_ready, 1)
            with act.Fori(0, STEPS) as i:
                for q, (a, z) in enumerate(quads):
                    act.wait_ge(flipped, i * len(quads) + (q + 1))
                    nc.scalar.copy(h[:, a:z, :], p_t[:, 0:z - a, :]).then_inc(h_ready, 1)


def tensor_edges(nc, d, c):
    a, b6, c6 = 10 ** -0.5, 30 ** -0.5, 2 * 30 ** -0.5
    with Stage(nc, "tp") as s:
        two = range(2)
        NT = NG * G
        attr = s.sb("attr", [P, NT, 9])
        mat = s.sb("mat", [P, NT, 3, 3])
        cols = [s.sb(f"cols{b}", [P, 4 * G], I32) for b in two]
        gat = [s.sb(f"gat{b}", [P, G, TPW]) for b in two]
        off = [s.sb(f"off{b}", [P, G]) for b in two]
        away = s.sb("away", [P, GE])
        pick = [s.sb(f"pick{b}", [P, G, P]) for b in two]
        msg = [s.sb(f"msg{b}", [P, G, 5, P]) for b in two]
        p_sum = [s.ps(f"p_sum{b}", [P, G, P]) for b in two]
        attr_in, passed, chained, offsets, awayed, picked, messages, summed, done = (
            s.sem(n) for n in ("attr_in", "passed", "chained", "offsets", "awayed", "picked", "messages", "summed",
                               "done"))
        ready = [s.sem(f"ready{b}") for b in two]
        gathered = [s.sem(f"gathered{b}") for b in two]
        block = s.block()

        @block.sync
        def _(sp):
            sp.dma_start(attr[:], d.attr).then_inc(attr_in, 16)
            with sp.Fori(0, NG // 2) as i:
                for b in two:
                    g = i * 2 + b
                    sp.wait_ge(done, (g + 1) * G)
                    sp.dma_start(cols[b][:], d.cols[bass.ds(g, 1), :, :]).then_inc(ready[b], 16)

        @block.gpsimd
        def _(pool):
            with pool.Fori(0, NG // 2) as i:
                for b in two:
                    pool.wait_ge(ready[b], (i + 1) * 16)
                    pool.sem_inc(passed, 1)
                    for t in range(G):
                        pool.indirect_dma_start(
                            gat[b][:, t, :], None, d.tp_rows,
                            bass.IndirectOffsetOnAxis(ap=cols[b][:, t:t + 1], axis=0)).then_inc(gathered[b], 16)

        @block.scalar
        def _(act):
            with act.Fori(0, NG // 2) as i:
                for b in two:
                    g = i * 2 + b
                    act.wait_ge(offsets, g + 1)
                    for t in range(G):
                        nc.scalar.activation(away[:, t * P:(t + 1) * P], c.iota[:], ACT.Abs,
                                             bias=off[b][:, t:t + 1]).then_inc(awayed, 1)
                    act.wait_ge(awayed, (g + 1) * G)
                    nc.scalar.activation(pick[b][:], away[:].rearrange("p (t e) -> p t e", t=G), ACT.Relu,
                                         scale=-1.0, bias=1.0).then_inc(picked, 1)
                    act.wait_ge(picked, g + 1)

        @block.vector
        def _(dve):
            count = [0]

            def chain(instruction):
                count[0] += 1
                instruction.then_inc(chained, 1)
                dve.wait_ge(chained, count[0])

            dve.sem_inc(done, 2 * G)
            chain(nc.vector.memset(c.acc[:, 0, :], 0.0))
            for b in two:
                chain(nc.vector.memset(msg[b][:, :, 4, 0:U], 0.0))
            dve.wait_ge(attr_in, 16)
            y2 = [attr[:, :, 4 + j] for j in range(5)]
            for i, k, j, f in ((0, 1, 1, a), (1, 0, 1, a), (0, 2, 0, a), (2, 0, 0, a), (1, 2, 3, a), (2, 1, 3, a),
                               (1, 1, 2, c6), (0, 0, 2, -b6), (2, 2, 2, -b6)):
                chain(nc.vector.tensor_scalar(mat[:, :, i, k], y2[j], f, None, ALU.mult))
            for i, f in ((0, -a), (2, a)):
                chain(nc.vector.scalar_tensor_tensor(mat[:, :, i, i], y2[4], f, mat[:, :, i, i], ALU.mult, ALU.add))
            with dve.Fori(0, NG // 2) as i:
                for b in two:
                    g = i * 2 + b
                    dve.wait_ge(ready[b], (i + 1) * 16)
                    nc.vector.tensor_tensor(off[b][:], cols[b][:, 2 * G:3 * G], cols[b][:, G:2 * G],
                                            ALU.subtract).then_inc(offsets, 1)
                    dve.wait_ge(gathered[b], (i + 1) * G * 16)
                    y = attr[:, bass.ds(g * G, G), :]
                    m = mat[:, bass.ds(g * G, G), :, :]
                    row, o = gat[b], msg[b]
                    nc.vector.tensor_tensor(o[:, :, 0, :], row[:, :, 0:D], bc(y[:, :, 0], 2, D),
                                            ALU.mult).then_inc(messages, 1)
                    nc.vector.tensor_tensor(o[:, :, 1, U:].rearrange("p t (w k) -> p t w k", k=3),
                                            bc(row[:, :, D:D + U], 3, 3), bc(y[:, :, 1:4], 2, U),
                                            ALU.mult).then_inc(messages, 1)
                    nc.vector.tensor_tensor(o[:, :, 1:4, 0:U],
                                            row[:, :, D + U:D + 4 * U].rearrange("p t (j w) -> p t j w", j=3),
                                            bc(y[:, :, 1:4], 3, U), ALU.mult).then_inc(messages, 1)
                    for j in range(3):
                        v = row[:, :, D + (4 + j) * U:D + (5 + j) * U]
                        nc.vector.tensor_tensor(o[:, :, 2 + j, U:].rearrange("p t (w k) -> p t w k", k=3),
                                                bc(v, 3, 3), bc(m[:, :, j, :], 2, U),
                                                ALU.mult).then_inc(messages, 1)
                for b in two:
                    g = i * 2 + b
                    dve.wait_ge(summed, g + 1)
                    for t in range(G):
                        base = dve.value_load(c.bases[0:1, bass.ds(g * G + t, 1)], min_val=0, max_val=NC - 1)
                        at = c.acc[:, 0, bass.ds(base, P)]
                        nc.vector.tensor_tensor(at, at, p_sum[b][:, t, :], ALU.add).then_inc(done, 1)
                        dve.wait_ge(done, g * G + (2 * G + t + 1))

        @block.tensor
        def _(pe):
            with pe.Fori(0, NG // 2) as i:
                for b in two:
                    g = i * 2 + b
                    pe.wait_ge(picked, g + 1)
                    pe.wait_ge(messages, (g + 1) * 6)
                    for t in range(G):
                        for k in range(5):
                            last = nc.tensor.matmul(p_sum[b][:, t, :], msg[b][:, t, k, :], pick[b][:, t, :],
                                                    start=k == 0, stop=k == 4)
                    last.then_inc(summed, 1)


class Dram:

    def __init__(self, args):
        self.x = args["x"]
        self.src = args["src"]
        self.dst = args["dst"]
        self.bases = args["bases"]
        self.cols = args["cols"]
        self.wcol = args["wcol"]
        self.attr = args["attr"]
        self.W_in = args["W_in"]
        self.b_in = args["b_in"]
        self.Wq = args["Wq"]
        self.bq = args["bq"]
        self.Wk = args["Wk"]
        self.bk = args["bk"]
        self.Wv = args["Wv"]
        self.bv = args["bv"]
        self.W2 = args["W2"]
        self.att_src = args["att_src"]
        self.att_dst = args["att_dst"]
        self.bias = args["bias"]
        self.gamma = args["gamma"]
        self.beta = args["beta"]
        self.w = [args[f"w{k}"] for k in range(5)]


class Chip:
    pass


def build(nc, args, out, upto=12):
    d, c = Dram(args), Chip()

    def scratch(name, shape):
        return nc.dram_tensor(f"scratch_{name}", shape, F32, kind="Internal").ap()

    d.A = scratch("A", (NC * NC + P,))
    d.brk = scratch("brk", (EP + 1,))
    d.key = scratch("key", (EP,))
    d.q_rows = scratch("q_rows", (NP, D))
    d.kv_rows = scratch("kv_rows", (NP, 2 * D))
    d.xw_rows = scratch("xw_rows", (NP, D + 4))
    d.dst_rows = scratch("dst_rows", (NP, 4))
    d.tp_rows = scratch("tp_rows", (NP, TPW))
    with Stage(nc, "all") as s:
        c.x = s.sb("x", [P, TW, D])
        c.acc = s.sb("acc", [P, 2, NP])
        c.bases = s.sb("bases", [1, NG * G], I32)
        c.ident = s.sb("ident", [P, P])
        c.lower = s.sb("lower", [P, P])
        c.iota = s.sb("iota", [P, P])
        c.pid = s.sb("pid", [P, 1])
        c.trash = s.sb("trash", [P, 1])
        steps = [lambda: prepare(nc, d, c),
                 lambda: attention_tables(nc, d, c),
                 lambda: softmax_edges(nc, d, c, "attn", 8, d.q_rows, d.kv_rows, D, c.acc, True),
                 lambda: finish_layer(nc, d, c, "fin0", divide=0.0, out=out if upto == 4 else None),
                 lambda: propagate(nc, d, c),
                 lambda: finish_layer(nc, d, c, "fin1", out=out if upto == 6 else None),
                 lambda: gat_tables(nc, d, c),
                 lambda: softmax_edges(nc, d, c, "gat", 4, d.dst_rows, d.xw_rows, 0, c.acc, False),
                 lambda: finish_layer(nc, d, c, "fin2", divide=1e-16, inner=(d.bias, d.gamma, d.beta),
                                      out=out if upto == 9 else None),
                 lambda: tensor_tables(nc, d, c),
                 lambda: tensor_edges(nc, d, c),
                 lambda: finish_layer(nc, d, c, "fin3", out=out)]
        for step in steps[:upto]:
            step()


def lay_out(inputs):
    a = {k: np.asarray(v) for k, v in inputs.items()}
    pad = EP - E
    src = np.concatenate([a["src"].astype(np.int32), np.arange(pad, dtype=np.int32)])
    dst = np.concatenate([a["dst"].astype(np.int32), np.full(pad, PAD_DST, np.int32)])
    w = np.concatenate([a["edge_weight"], np.zeros(pad, np.float32)])
    attr = np.concatenate([a["edge_attr_9"], np.zeros((pad, 9), np.float32)])
    x = np.concatenate([a["x"], np.zeros((NP - N, D), np.float32)])

    def by_group(v):
        return v.reshape(NG, G, P).transpose(0, 2, 1)

    bases = dst[::P]
    after = np.concatenate([dst[1:], np.full(1, NC, np.int32)])
    cols = np.concatenate([by_group(src), by_group(dst), by_group(np.repeat(bases, P)), by_group(after)], axis=2)
    arrays = {
        "x": x, "src": src, "dst": np.concatenate([np.full(1, -1, np.int32), dst, np.full(1, NC, np.int32)]),
        "bases": bases.reshape(1, -1), "cols": cols, "wcol": by_group(w),
        "attr": attr.reshape(NG * G, P, 9).transpose(1, 0, 2),
        "W_in": a["L0_gnn_W_in"], "b_in": a["L0_gnn_b_in"], "Wq": a["L0_gnn_Wq"], "bq": a["L0_gnn_bq"],
        "Wk": a["L0_gnn_Wk"], "bk": a["L0_gnn_bk"], "Wv": a["L0_gnn_Wv"], "bv": a["L0_gnn_bv"],
        "W2": a["L2_gnn_W"], "att_src": a["L2_gnn_att_src"], "att_dst": a["L2_gnn_att_dst"],
        "bias": a["L2_gnn_bias"], "gamma": a["L2_gnn_gamma"], "beta": a["L2_gnn_beta"],
        **{f"w{k}": a[f"L3_gnn_w{k}"].reshape(U, U) for k in range(5)},
    }
    return {k: np.ascontiguousarray(v) for k, v in arrays.items()}


def kernel(**inputs):
    import concourse.bacc as bacc
    from concourse.bass_utils import run_bass_kernel_spmd

    nc = bacc.Bacc("TRN2", target_bir_lowering=False, num_devices=1)
    arrays = lay_out(inputs)
    args = {k: nc.dram_tensor(f"in_{k}", v.shape, mybir.dt.from_np(v.dtype), kind="ExternalInput").ap()
            for k, v in arrays.items()}
    out = nc.dram_tensor("out", (N, D), F32, kind="ExternalOutput").ap()
    build(nc, args, out)
    result = run_bass_kernel_spmd(nc, [{f"in_{k}": v for k, v in arrays.items()}], core_ids=[0])
    return result.results[0]["out"]
```
